# Optimizing a Trainium2 kernel written in Bass

```python
import numpy as np
import jax
import jax.numpy as jnp

def _softmax(x, axis=-1):
    return jax.nn.softmax(x, axis=axis)

def _gelu(x):
    return jax.nn.gelu(x, approximate=True)

def _silu(x):
    return jax.nn.silu(x)

def _sigmoid(x):
    return jax.nn.sigmoid(x)

def _layernorm(x, axis=-1, eps=1e-05):
    m = jnp.mean(x, axis=axis, keepdims=True)
    v = jnp.var(x, axis=axis, keepdims=True)
    return (x - m) / jnp.sqrt(v + eps)

def _scatter_add(tgt, idx, src, axis=0):
    return tgt.at[idx].add(src)

def _segment_sum(src, seg, n):
    return jax.ops.segment_sum(src, seg, n)
kernel_name = 'mk_adaln_ffn_d1_seqx_r8_ebaed3'

def setup_inputs(seed: int=0):
    np.random.seed(seed)
    _w = jnp.asarray

    def _rec_inputs():
        import jax
        import jax.numpy as jnp
        _rk = jax.random.key(seed)
        x = -0.000125 + 0.9999 * jax.random.normal(jax.random.fold_in(_rk, 1), (8, 128, 512), jnp.float32)
        _lenS = 128 - jax.random.randint(jax.random.fold_in(_rk, 7), (8,), 0, max(1, 128 // 4) + 1, jnp.int32)
        _lenS2 = 128 - jax.random.randint(jax.random.fold_in(_rk, 8), (8,), 0, max(1, 128 // 4) + 1, jnp.int32)
        itok_B_0_7 = jax.random.randint(jax.random.fold_in(_rk, 11), (8,), 0, 8, jnp.int32)
        return (x, itok_B_0_7)
    x, itok_B_0_7 = _rec_inputs()

    def _L0_cond_setup():
        import jax, jax.numpy as jnp
        import numpy as np
        TOP_K = 2
        LANG_BIAS = 5.0
        SCALING = 32.0 / 16.0
        LANGUAGE_PAD_ID = -1
        key = jax.random.key(seed)
        ks = jax.random.split(key, 6)
        B, T, D, O, E, R = (4, 256, 512, 512, 8, 16)
        x = jax.random.normal(ks[0], (B, T, D), dtype=jnp.float32)
        language_ids = jax.random.randint(ks[1], (B,), 0, E).astype(jnp.int64)
        W = jax.random.normal(ks[2], (O, D), dtype=jnp.float32) * (1.0 / np.sqrt(D))
        Wr = jax.random.normal(ks[3], (E, D), dtype=jnp.float32) * (1.0 / np.sqrt(D))
        A = jax.random.normal(ks[4], (E, R, D), dtype=jnp.float32) * (1.0 / np.sqrt(D))
        Bm = jax.random.normal(ks[5], (O, R), dtype=jnp.float32) * 0.0
        Bm = jnp.broadcast_to(Bm, (E, O, R)) + jax.random.normal(ks[5], (E, O, R), dtype=jnp.float32) * 0.02
        return {'x': x, 'language_ids': language_ids, 'W': W, 'Wr': Wr, 'A': A, 'B': Bm}
    _L0_cond_all = _L0_cond_setup()
    _L0_cond_in = {k: v for k, v in _L0_cond_all.items() if k in ('W', 'Wr', 'A', 'B')}
    del _L0_cond_all

    def _L0_ffn_setup():
        import jax, jax.numpy as jnp
        import numpy as np
        B, S, D, O, E, R = (2, 512, 512, 512, 8, 16)
        TOP_K = 2
        SCALING = 32.0 / 16.0
        key = jax.random.key(seed)
        k = jax.random.split(key, 6)
        x = jax.random.normal(k[0], (B, S, D), dtype=jnp.float32)
        W_base = jax.random.normal(k[1], (O, D), dtype=jnp.float32) * 0.02
        b_base = jax.random.normal(k[2], (O,), dtype=jnp.float32) * 0.02
        W_router = jax.random.normal(k[3], (E, D), dtype=jnp.float32) * 0.01
        lora_A = jax.random.normal(k[4], (E, R, D), dtype=jnp.float32) * (1.0 / np.sqrt(D))
        lora_B = jax.random.normal(k[5], (E, O, R), dtype=jnp.float32) * 0.02
        return {'x': x, 'W_base': W_base, 'b_base': b_base, 'W_router': W_router, 'lora_A': lora_A, 'lora_B': lora_B}
    _L0_ffn_all = _L0_ffn_setup()
    _L0_ffn_in = {k: v for k, v in _L0_ffn_all.items() if k in ('W_base', 'b_base', 'W_router', 'lora_A', 'lora_B')}
    del _L0_ffn_all
    return {'x': x, 'itok_B_0_7': itok_B_0_7, 'L0_cond_W': _L0_cond_in['W'], 'L0_cond_Wr': _L0_cond_in['Wr'], 'L0_cond_A': _L0_cond_in['A'], 'L0_cond_B': _L0_cond_in['B'], 'L0_ffn_W_base': _L0_ffn_in['W_base'], 'L0_ffn_b_base': _L0_ffn_in['b_base'], 'L0_ffn_W_router': _L0_ffn_in['W_router'], 'L0_ffn_lora_A': _L0_ffn_in['lora_A'], 'L0_ffn_lora_B': _L0_ffn_in['lora_B']}

def reference(x, itok_B_0_7, L0_cond_W, L0_cond_Wr, L0_cond_A, L0_cond_B, L0_ffn_W_base, L0_ffn_b_base, L0_ffn_W_router, L0_ffn_lora_A, L0_ffn_lora_B):
    import jax
    import jax.numpy as jnp

    def _L0_cond_ref(x, language_ids, W, Wr, A, B):
        import jax, jax.numpy as jnp
        import numpy as np
        TOP_K = 2
        LANG_BIAS = 5.0
        SCALING = 32.0 / 16.0
        LANGUAGE_PAD_ID = -1
        base = jnp.einsum('btd,od->bto', x, W)
        E = Wr.shape[0]
        logits = jnp.einsum('btd,ed->bte', x.astype(jnp.float32), Wr.astype(jnp.float32))
        expert_targets = language_ids
        valid = expert_targets >= 0
        tgt = jnp.where(valid, expert_targets, 0)
        bias = jax.nn.one_hot(tgt, E, dtype=logits.dtype) * LANG_BIAS
        bias = jnp.where(valid[:, None], bias, 0.0)
        logits = logits + bias[:, None, :]
        topw, topi = jax.lax.top_k(logits, TOP_K)
        weights = jax.nn.softmax(topw, axis=-1)
        gates = jnp.sum(jax.nn.one_hot(topi, E, dtype=weights.dtype) * weights[..., None], axis=-2)
        gates = gates.astype(x.dtype)
        h = jnp.einsum('btd,erd->bter', x, A)
        lora_out = jnp.einsum('bter,bte,eor->bto', h, gates, B)
        return base + SCALING * lora_out

    def _L0_ffn_ref(x, W_base, b_base, W_router, lora_A, lora_B):
        import jax, jax.numpy as jnp
        import numpy as np
        B, S, D, O, E, R = (2, 512, 512, 512, 8, 16)
        TOP_K = 2
        SCALING = 32.0 / 16.0
        d = x.shape[-1]
        n_experts = W_router.shape[0]
        xf = x.reshape(-1, d)
        logits = xf @ W_router.T
        probs = jax.nn.softmax(logits, axis=-1)
        topk_p, topk_i = jax.lax.top_k(probs, TOP_K)
        topk_p = topk_p / jnp.sum(topk_p, axis=-1, keepdims=True)
        w = jnp.sum(jax.nn.one_hot(topk_i, n_experts, dtype=xf.dtype) * topk_p[..., None], axis=1)
        h = jnp.einsum('td,erd->ter', xf, lora_A)
        lora_out = jnp.einsum('ter,eor,te->to', h, lora_B, w) * SCALING
        base = x @ W_base.T + b_base
        return base + lora_out.reshape(x.shape[:-1] + (W_base.shape[0],))
    x = x + _L0_ffn_ref(_L0_cond_ref(x, itok_B_0_7, L0_cond_W, L0_cond_Wr, L0_cond_A, L0_cond_B), L0_ffn_W_base, L0_ffn_b_base, L0_ffn_W_router, L0_ffn_lora_A, L0_ffn_lora_B)
    return x

_drawn_inputs = setup_inputs


def setup_inputs(seed=0):
    import zlib

    import numpy as np

    out = dict(_drawn_inputs(seed))
    spreads = {}
    factors = {'L0_cond_Wr': 5.043, 'L0_ffn_b_base': 3.147}
    for name, (base, spread) in spreads.items():
        noise = np.random.default_rng([zlib.crc32(name.encode()), seed]).standard_normal(out[name].shape)
        drawn = base * np.exp(spread * noise) if base else spread * noise
        out[name] = jnp.asarray(drawn.astype(out[name].dtype))
    for name, factor in factors.items():
        out[name] = (out[name] * factor).astype(out[name].dtype)
    return out
```

```python
from contextlib import ExitStack

import concourse.bass as bass
from concourse import mybir

F32 = mybir.dt.float32
F32R = mybir.dt.float32r
BF16 = mybir.dt.bfloat16
I32 = mybir.dt.int32
ALU = mybir.AluOpType
ACT = mybir.ActivationFunctionType
AX_X = mybir.AxisListType.X

P = 128
TILES = 8
TOKENS = TILES * P
D = 512
KC = D // P
E, R = 8, 16
ER = E * R
ROUTED = ER + E
M_COLS = D + ROUTED
S_COLS = D + ER
BLOCKS = KC + 1
HALF_A = 3 * P
HALVES = ((0, HALF_A), (HALF_A, M_COLS))
R_COLS = M_COLS + ROUTED
PAIR = 2 * ROUTED
GROUPS = 4
GT = TOKENS // GROUPS
BANK = 512
SCALING = 2.0
LANG_BIAS = 5.0
WARM_UP = 9


def adaln_ffn(nc: bass.Bass, wm, ar, xt, b2, bias, ids, out):
    with ExitStack() as ctx:
        def sb(name, shape, dt=F32):
            return ctx.enter_context(nc.sbuf_tensor(name, shape, dt))

        def sem(name):
            return ctx.enter_context(nc.semaphore(name))

        wm_f = sb("wm_f", [P, KC, S_COLS + M_COLS])
        wm_hi = sb("wm_hi", [P, KC, S_COLS + M_COLS], F32R)
        wm_lo = sb("wm_lo", [P, KC, S_COLS + M_COLS], F32R)
        ar_f = sb("ar_f", [P, KC, ROUTED])
        b2_f = sb("b2_f", [P, D])
        b2_hi = sb("b2_hi", [P, D], F32R)
        b2_lo = sb("b2_lo", [P, D], F32R)
        bias_all = sb("bias_all", [P, D])
        x_f = sb("x_f", [P, GROUPS, KC, GT])
        x_hi = sb("x_hi", [P, GROUPS, KC, GT], F32R)
        x_lo = sb("x_lo", [P, GROUPS, KC, GT], F32R)
        r_hi = sb("r_hi", [P, KC, R_COLS], F32R)
        r_lo = sb("r_lo", [P, KC, R_COLS], F32R)
        bm_hi = sb("bm_hi", [P, M_COLS], F32R)
        bm_lo = sb("bm_lo", [P, M_COLS], F32R)
        narrow = sb("narrow", [P, TILES, PAIR])
        hg = sb("hg", [P, TILES, ER])
        hgt_hi = [sb(f"hgt{n}_hi", [P, TOKENS], F32R) for n in (1, 2)]
        hgt_lo = [sb(f"hgt{n}_lo", [P, TOKENS], F32R) for n in (1, 2)]
        ids_all = sb("ids_all", [P, TILES], I32)
        expert = sb("expert", [P, TILES, E], I32)
        is_lang = sb("is_lang", [P, TILES, E])
        not_first = sb("not_first", [P, TILES, E])
        logits = sb("logits", [P, TILES, E])
        top = sb("top", [P, TILES, 8])
        at_second = sb("at_second", [P, TILES, E])
        nth_equal = sb("nth_equal", [P, TILES, E])
        tied = sb("tied", [P, TILES])
        chosen = sb("chosen", [P, TILES, E])
        above = sb("above", [P, TILES, E])
        below_max = sb("below_max", [P, TILES, E])
        exps = sb("exps", [P, TILES, E])
        total = sb("total", [P, TILES])
        gates = sb("gates", [P, TILES, E])
        ident = sb("ident", [P, P])
        zeros = sb("zeros", [P, BANK], BF16)
        sums = x_f[:, :, :, :].rearrange("p g k t -> p (g k t)").rearrange("p (t o) -> p t o", t=TILES)

        ps = ctx.enter_context(nc.psum_tensor("ps", [P, 8, BANK], F32))

        wm_in = [sem(f"wm_in{k}") for k in range(KC)]
        wm0_m_in = sem("wm0_m_in")
        ar_in, b2_in, bias_in, ids_in = sem("ar_in"), sem("b2_in"), sem("bias_in"), sem("ids_in")
        x_in = [sem(f"x_in{g}") for g in range(GROUPS)]
        wm_hi_done, wm_lo_done = sem("wm_hi_done"), sem("wm_lo_done")
        ar_hi_done, ar_lo_done = sem("ar_hi_done"), sem("ar_lo_done")
        x_hi_done, x_lo_done = sem("x_hi_done"), sem("x_lo_done")
        b2_hi_done, b2_lo_done = sem("b2_hi_done"), sem("b2_lo_done")
        c_hi_done, c_lo_done = sem("c_hi_done"), sem("c_lo_done")
        hgt_hi_done, hgt_lo_done = sem("hgt_hi_done"), sem("hgt_lo_done")
        c_summed, c_plus_i = sem("c_summed"), sem("c_plus_i")
        narrow_summed, narrow_copied = sem("narrow_summed"), sem("narrow_copied")
        base_summed, base_copied = sem("base_summed"), sem("base_copied")
        hg_turned, second_summed = sem("hg_turned"), sem("second_summed")
        lora_summed, tile_done = sem("lora_summed"), sem("tile_done")
        zeros_set, ident_zeroed, ident_set, expert_set = (sem("zeros_set"), sem("ident_zeroed"),
                                                          sem("ident_set"), sem("expert_set"))
        route_step, below_max_done, exps_done, hg_done = (sem("route_step"), sem("below_max_done"),
                                                          sem("exps_done"), sem("hg_done"))
        stored = sem("stored")

        pieces = [(0, 0, S_COLS), (0, S_COLS, S_COLS + M_COLS)]
        pieces += [(k, 0, S_COLS + M_COLS) for k in range(1, KC)]

        def pieces_to(k):
            return k + 2

        block_banks = [(0, 1), (2, 3), (4, 5), (6, 7), (0, 1)]
        narrow_banks = (2, 3)
        wide_banks = (4, 5, 6, 7)
        turned_banks = ((0, 1), (1, 2))
        second_banks = (2, 3, 0)
        second_tiles = ((0, 3), (3, 6), (6, TILES))
        PER_TURN = BANK // P

        block = ctx.enter_context(nc.Block())

        @block.sync
        def _(sp):
            sp.dma_start(wm_f[:, 0, 0:S_COLS], wm[0, :, 0:S_COLS]).then_inc(wm_in[0], 16)
            sp.dma_start(wm_f[:, 0, S_COLS:], wm[0, :, S_COLS:]).then_inc(wm0_m_in, 16)
            for k in range(1, KC):
                sp.dma_start(wm_f[:, k, :], wm[k]).then_inc(wm_in[k], 16)
            sp.dma_start(x_f[:, 0], xt[0]).then_inc(x_in[0], 16)
            sp.dma_start(ar_f[:, :, :], ar).then_inc(ar_in, 16)
            for g in range(1, GROUPS):
                sp.dma_start(x_f[:, g], xt[g]).then_inc(x_in[g], 16)
            sp.dma_start(ids_all[:, :], ids.to_broadcast([P, TILES])).then_inc(ids_in, 16)
            sp.dma_start(bias_all[:, :], bias.to_broadcast([P, D])).then_inc(bias_in, 16)
            sp.dma_start(b2_f[:, :], b2).then_inc(b2_in, 16)
            for t in range(TILES):
                sp.wait_ge(tile_done, t + 1)
                sp.dma_start(out[t], sums[:, t, :]).then_inc(stored, 16)
            sp.wait_ge(stored, 16 * TILES)

        @block.gpsimd
        def _(pool):
            nc.gpsimd.memset(ident[:, :], 0.0).then_inc(ident_zeroed, 1)
            nc.gpsimd.iota(expert[:, :, :], pattern=[[0, TILES], [1, E]], base=0,
                           channel_multiplier=0).then_inc(expert_set, 1)
            pool.wait_ge(ident_zeroed, 1)
            nc.gpsimd.affine_select(out=ident[:, :], in_=ident[:, :], compare_op=ALU.not_equal, fill=1.0,
                                    base=0, pattern=[[-1, P]], channel_multiplier=1).then_inc(ident_set, 1)

        @block.scalar
        def _(act):
            for n, (k, a, b) in enumerate(pieces):
                act.wait_ge(wm0_m_in if n == 1 else wm_in[k], 16)
                nc.scalar.copy(wm_hi[:, k, a:b], wm_f[:, k, a:b]).then_inc(wm_hi_done, 1)
            act.wait_ge(x_in[0], 16)
            nc.scalar.copy(x_hi[:, 0], x_f[:, 0]).then_inc(x_hi_done, 1)
            act.wait_ge(ar_in, 16)
            nc.scalar.copy(r_hi[:, :, M_COLS:], ar_f[:, :, :]).then_inc(ar_hi_done, 1)
            for g in range(1, GROUPS):
                act.wait_ge(x_in[g], 16)
                nc.scalar.copy(x_hi[:, g], x_f[:, g]).then_inc(x_hi_done, 1)
            act.wait_ge(b2_in, 16)
            nc.scalar.copy(b2_hi[:, :], b2_f[:, :]).then_inc(b2_hi_done, 1)
            for b, banks in enumerate(block_banks):
                if b < KC:
                    act.wait_ge(c_plus_i, b + 1)
                else:
                    act.wait_ge(c_summed, b + 1)
                for bank, (lo, hi) in zip(banks, HALVES):
                    dst = r_hi[:, b, lo:hi] if b < KC else bm_hi[:, lo:hi]
                    nc.scalar.copy(dst, ps[:, bank, 0:hi - lo]).then_inc(c_hi_done, 1)
            for t in range(TILES):
                act.wait_ge(narrow_summed, t + 1)
                nc.scalar.copy(narrow[:, t, :], ps[:, narrow_banks[t % 2], 0:PAIR]).then_inc(narrow_copied, 1)
            for n in range(2):
                act.wait_ge(below_max_done, n + 1)
                nc.scalar.activation(exps[:, :, :], below_max[:, :, :], ACT.Exp).then_inc(exps_done, 1)
                for q in range(2):
                    act.wait_ge(hg_turned, 2 * n + q + 1)
                    nc.scalar.copy(hgt_hi[n][:, q * BANK:(q + 1) * BANK],
                                   ps[:, turned_banks[n][q], :]).then_inc(hgt_hi_done, 1)

        @block.vector
        def _(dve):
            nc.vector.memset(zeros[:, :], 0.0).then_inc(zeros_set, 1)
            for n, (k, a, b) in enumerate(pieces):
                dve.wait_ge(wm_hi_done, n + 1)
                nc.vector.tensor_tensor(wm_lo[:, k, a:b], wm_f[:, k, a:b],
                                        wm_hi[:, k, a:b].bitcast(F32), ALU.subtract).then_inc(wm_lo_done, 1)

            def x_low(g):
                dve.wait_ge(x_hi_done, g + 1)
                nc.vector.tensor_tensor(x_lo[:, g], x_f[:, g], x_hi[:, g].bitcast(F32),
                                        ALU.subtract).then_inc(x_lo_done, 1)

            x_low(0)
            dve.wait_ge(ar_hi_done, 1)
            nc.vector.tensor_tensor(r_lo[:, :, M_COLS:], ar_f[:, :, :], r_hi[:, :, M_COLS:].bitcast(F32),
                                    ALU.subtract).then_inc(ar_lo_done, 1)
            for g in range(1, GROUPS):
                x_low(g)
            dve.wait_ge(b2_hi_done, 1)
            nc.vector.tensor_tensor(b2_lo[:, :], b2_f[:, :], b2_hi[:, :].bitcast(F32),
                                    ALU.subtract).then_inc(b2_lo_done, 1)

            dve.wait_ge(ident_set, 1)
            for b, banks in enumerate(block_banks):
                dve.wait_ge(c_summed, b + 1)
                if b < KC:
                    half = 0 if b * P < HALF_A else 1
                    at = b * P - HALVES[half][0]
                    diagonal = ps[:, banks[half], at:at + P]
                    nc.vector.tensor_tensor(diagonal, diagonal, ident[:, :], ALU.add).then_inc(c_plus_i, 1)
                for h, (bank, (lo, hi)) in enumerate(zip(banks, HALVES)):
                    high = r_hi[:, b, lo:hi] if b < KC else bm_hi[:, lo:hi]
                    low = r_lo[:, b, lo:hi] if b < KC else bm_lo[:, lo:hi]
                    dve.wait_ge(c_hi_done, 2 * b + h + 1)
                    nc.vector.tensor_tensor(low, ps[:, bank, 0:hi - lo], high.bitcast(F32),
                                            ALU.subtract).then_inc(c_lo_done, 1)

            steps = [0]

            def then(ins):
                steps[0] += 1
                ins.then_inc(route_step, 1)
                dve.wait_ge(route_step, steps[0])

            def per_tile(a):
                return a.to_broadcast([P, TILES, E])

            dve.wait_ge(expert_set, 1)
            dve.wait_ge(ids_in, 16)
            nc.vector.tensor_scalar(not_first[:, :, :], expert[:, :, :], 0.0, None, ALU.is_gt)
            then(nc.vector.tensor_tensor(is_lang[:, :, :], expert[:, :, :],
                                         per_tile(ids_all[:, :].unsqueeze(2)), ALU.is_equal))

            def route(n):
                for t in range(TILES):
                    last = nc.vector.max(top[:, t, :], logits[:, t, :])
                then(last)
                first, second = per_tile(top[:, :, 0:1]), per_tile(top[:, :, 1:2])
                nc.vector.tensor_tensor(below_max[:, :, :], logits[:, :, :], first,
                                        ALU.subtract).then_inc(below_max_done, 1)
                nc.vector.tensor_tensor(tied[:, :].unsqueeze(2), top[:, :, 0:1], top[:, :, 1:2], ALU.is_equal)
                nc.vector.tensor_tensor(above[:, :, :], logits[:, :, :], second, ALU.is_gt)
                then(nc.vector.tensor_tensor(at_second[:, :, :], logits[:, :, :], second, ALU.is_equal))
                flat = "p t e -> p (t e)"
                then(nc.vector.tensor_tensor_scan(
                    nth_equal[:, :, :].rearrange(flat), not_first[:, :, :].rearrange(flat),
                    at_second[:, :, :].rearrange(flat), 0.0, ALU.mult, ALU.add))
                then(nc.vector.scalar_tensor_tensor(chosen[:, :, :], nth_equal[:, :, :], -1.0,
                                                    per_tile(tied[:, :].unsqueeze(2)), ALU.add, ALU.is_le))
                then(nc.vector.tensor_tensor(chosen[:, :, :], chosen[:, :, :], at_second[:, :, :], ALU.mult))
                then(nc.vector.tensor_tensor(chosen[:, :, :], chosen[:, :, :], above[:, :, :], ALU.add))
                dve.wait_ge(exps_done, n + 1)
                then(nc.vector.tensor_tensor(chosen[:, :, :], chosen[:, :, :], exps[:, :, :], ALU.mult))
                then(nc.vector.tensor_reduce(total[:, :], chosen[:, :, :], AX_X, ALU.add))
                then(nc.vector.reciprocal(total[:, :], total[:, :]))
                then(nc.vector.scalar_tensor_tensor(gates[:, :, :], chosen[:, :, :], SCALING,
                                                    per_tile(total[:, :].unsqueeze(2)), ALU.mult, ALU.mult))

            def gated(n, first_col):
                for q in range(2):
                    t0, t1 = q * PER_TURN, (q + 1) * PER_TURN
                    if n:
                        dve.wait_ge(hg_turned, q + 1)
                    h = narrow[:, t0:t1, first_col:first_col + ER].rearrange("p t (e r) -> p t e r", e=E)
                    nc.vector.tensor_tensor(
                        hg[:, t0:t1, :].rearrange("p t (e r) -> p t e r", e=E), h,
                        gates[:, t0:t1, :].unsqueeze(3).to_broadcast([P, PER_TURN, E, R]),
                        ALU.mult).then_inc(hg_done, 1)

            def hgt_low(n):
                for q in range(2):
                    cols = slice(q * BANK, (q + 1) * BANK)
                    dve.wait_ge(hgt_hi_done, 2 * n + q + 1)
                    nc.vector.tensor_tensor(hgt_lo[n][:, cols], ps[:, turned_banks[n][q], :],
                                            hgt_hi[n][:, cols].bitcast(F32), ALU.subtract).then_inc(hgt_lo_done, 1)

            def base_out(t):
                dve.wait_ge(base_summed, t + 1)
                nc.vector.tensor_tensor(sums[:, t, :], ps[:, wide_banks[t % 4], :], bias_all[:, :],
                                        ALU.add).then_inc(base_copied, 1)

            dve.wait_ge(narrow_copied, TILES)
            then(nc.vector.scalar_tensor_tensor(logits[:, :, :], is_lang[:, :, :], LANG_BIAS,
                                                narrow[:, :, ROUTED + ER:], ALU.mult, ALU.add))
            route(0)
            gated(0, ROUTED)
            dve.wait_ge(bias_in, 16)
            dve.wait_ge(x_lo_done, GROUPS)
            base_out(0)
            hgt_low(0)
            base_out(1)
            for n, (t0, t1) in enumerate(second_tiles):
                dve.wait_ge(second_summed, n + 1)
                part = ps[:, second_banks[n], 0:(t1 - t0) * ROUTED].rearrange("p (t c) -> p t c", c=ROUTED)
                mine = narrow[:, t0:t1, 0:ROUTED]
                then(nc.vector.tensor_tensor(mine, part, mine, ALU.add))
            then(nc.vector.tensor_copy(logits[:, :, :], narrow[:, :, ER:ROUTED]))
            route(1)
            gated(1, 0)
            for t in range(2, 6):
                base_out(t)
            hgt_low(1)
            for t in range(6, TILES):
                base_out(t)
            for t in range(TILES):
                dve.wait_ge(lora_summed, t + 1)
                dve.wait_ge(base_copied, t + 1)
                nc.vector.tensor_tensor(sums[:, t, :], ps[:, wide_banks[t % 4], :], sums[:, t, :],
                                        ALU.add).then_inc(tile_done, 1)

        @block.tensor
        def _(pe):
            pe.wait_ge(zeros_set, 1)
            for _ in range(WARM_UP):
                nc.tensor.matmul(ps[:, 7, :], zeros[:, 0:P], zeros[:, :], start=True, stop=True)

            def folding(b, k, low_s, low_m, first, last):
                s = (wm_lo if low_s else wm_hi)[:, k, b * P:(b + 1) * P]
                m = wm_lo if low_m else wm_hi
                for bank, (lo, hi) in zip(block_banks[b], HALVES):
                    mm = nc.tensor.matmul(ps[:, bank, 0:hi - lo], s, m[:, k, S_COLS + lo:S_COLS + hi],
                                          start=first, stop=last)
                if last:
                    mm.then_inc(c_summed, 1)

            passes = ((False, False), (False, True), (True, False))

            for k in range(KC):
                pe.wait_ge(wm_hi_done, pieces_to(k))
                if k < KC - 1:
                    for n, (low_s, low_m) in enumerate(passes):
                        if n == 1:
                            pe.wait_ge(wm_lo_done, pieces_to(k))
                        for b in range(3):
                            folding(b, k, low_s, low_m, k == 0 and n == 0, False)
                else:
                    pe.wait_ge(wm_lo_done, pieces_to(k))
                    for b in range(3):
                        for n, (low_s, low_m) in enumerate(passes):
                            folding(b, k, low_s, low_m, False, n == 2)
            for b in (3, 4):
                if b == 4:
                    pe.wait_ge(c_lo_done, 2)
                for k in range(KC):
                    for n, (low_s, low_m) in enumerate(passes):
                        folding(b, k, low_s, low_m, k == 0 and n == 0, k == KC - 1 and n == 2)

            def x_part(part, t, k):
                g, at = t * P // GT, t * P % GT
                return part[:, g, k, at:at + P]

            def x_product(dst, t, a, b):
                for k in range(KC):
                    if t == 0:
                        pe.wait_ge(c_lo_done, 2 * (k + 1))
                    for n, (low_x, low_r) in enumerate(passes):
                        mm = nc.tensor.matmul(dst, x_part(x_lo if low_x else x_hi, t, k),
                                              (r_lo if low_r else r_hi)[:, k, a:b],
                                              start=(k == 0 and n == 0), stop=(k == KC - 1 and n == 2))
                return mm

            pe.wait_ge(ar_lo_done, 1)
            for t in range(TILES):
                if t % 2 == 0:
                    pe.wait_ge(x_lo_done, t // 2 + 1)
                if t < 2:
                    pe.wait_ge(c_lo_done, 4)
                else:
                    pe.wait_ge(narrow_copied, t - 1)
                x_product(ps[:, narrow_banks[t % 2], 0:PAIR], t, D, R_COLS).then_inc(narrow_summed, 1)

            def base(t):
                if t < 4:
                    pe.wait_ge(c_lo_done, 2 * KC)
                else:
                    pe.wait_ge(base_copied, t - 3)
                x_product(ps[:, wide_banks[t % 4], :], t, 0, D).then_inc(base_summed, 1)

            def turn(n):
                for q in range(2):
                    pe.wait_ge(hg_done, 2 * n + q + 1)
                    if n == 0:
                        pe.wait_ge(c_lo_done, 2 * BLOCKS)
                    else:
                        pe.wait_ge(hgt_lo_done, 2)
                    for t in range(q * PER_TURN, (q + 1) * PER_TURN):
                        at = (t % PER_TURN) * P
                        mm = nc.tensor.transpose(ps[:, turned_banks[n][q], at:at + P], hg[:, t, :], ident[:, :])
                    mm.then_inc(hg_turned, 1)

            def hgt_product(dst, n, t, high, low, first, last):
                for i, (low_h, low_m) in enumerate(passes):
                    mm = nc.tensor.matmul(dst, (hgt_lo if low_h else hgt_hi)[n][:, t * P:(t + 1) * P],
                                          low if low_m else high, start=(first and i == 0), stop=(last and i == 2))
                return mm

            base(0)
            base(1)
            turn(0)
            base(2)
            pe.wait_ge(narrow_copied, TILES)
            pe.wait_ge(hgt_lo_done, 2)
            for n, (t0, t1) in enumerate(second_tiles):
                for t in range(t0, t1):
                    at = (t - t0) * ROUTED
                    mm = hgt_product(ps[:, second_banks[n], at:at + ROUTED], 0, t,
                                     bm_hi[:, D:], bm_lo[:, D:], True, True)
                mm.then_inc(second_summed, 1)
            for t in range(3, 6):
                base(t)
            turn(1)
            for t in range(6, TILES):
                base(t)
            pe.wait_ge(b2_lo_done, 1)
            pe.wait_ge(hgt_lo_done, 4)
            for t in range(TILES):
                if t < 4:
                    pe.wait_ge(base_copied, t + 5)
                else:
                    pe.wait_ge(tile_done, t - 3)
                dst = ps[:, wide_banks[t % 4], :]
                hgt_product(dst, 0, t, bm_hi[:, 0:D], bm_lo[:, 0:D], True, False)
                hgt_product(dst, 1, t, b2_hi[:, :], b2_lo[:, :], False, True).then_inc(lora_summed, 1)


def kernel(x, itok_B_0_7, L0_cond_W, L0_cond_Wr, L0_cond_A, L0_cond_B, L0_ffn_W_base, L0_ffn_b_base,
           L0_ffn_W_router, L0_ffn_lora_A, L0_ffn_lora_B):
    import numpy as np
    import concourse.bacc as bacc
    from concourse.bass_utils import run_bass_kernel_spmd

    def a(v):
        return np.asarray(v)

    b1_rows = a(L0_cond_B).transpose(1, 0, 2).reshape(D, ER)
    wm = np.concatenate([a(L0_cond_W), b1_rows, a(L0_ffn_W_base).T, a(L0_ffn_lora_A).reshape(ER, D).T,
                         a(L0_ffn_W_router).T], axis=1).reshape(KC, P, S_COLS + M_COLS)
    ar = np.concatenate([a(L0_cond_A).reshape(ER, D).T, a(L0_cond_Wr).T], axis=1)
    arrays = {
        "wm": wm,
        "ar": ar.reshape(KC, P, ROUTED).transpose(1, 0, 2),
        "xt": a(x).reshape(GROUPS, GT, KC, P).transpose(0, 3, 2, 1),
        "b2": a(L0_ffn_lora_B).transpose(0, 2, 1).reshape(ER, D),
        "bias": a(L0_ffn_b_base).reshape(1, D),
        "ids": a(itok_B_0_7).reshape(1, TILES),
    }
    arrays = {name: np.ascontiguousarray(v) for name, v in arrays.items()}
    nc = bacc.Bacc("TRN2", target_bir_lowering=False, num_devices=1)
    args = [nc.dram_tensor(name, v.shape, mybir.dt.from_np(v.dtype), kind="ExternalInput").ap()
            for name, v in arrays.items()]
    out = nc.dram_tensor("out", (TILES, P, D), F32, kind="ExternalOutput").ap()
    adaln_ffn(nc, *args, out)
    result = run_bass_kernel_spmd(nc, [arrays], core_ids=[0])
    return result.results[0]["out"]
```

```python
from contextlib import ExitStack

import concourse.bass as bass
from concourse import mybir

F32 = mybir.dt.float32
F32R = mybir.dt.float32r
BF16 = mybir.dt.bfloat16
I32 = mybir.dt.int32
ALU = mybir.AluOpType
ACT = mybir.ActivationFunctionType
AX_X = mybir.AxisListType.X

P = 128
TILES = 8
TOKENS = TILES * P
D = 512
KC = D // P
E, R = 8, 16
ER = E * R
ROUTED = ER + E
M_COLS = D + ROUTED
BLOCKS = KC + 1
EARLY = 3
S_EARLY = EARLY * P
S_LATE = BLOCKS * P - S_EARLY
HALF_A = 3 * P
HALVES = ((0, HALF_A), (HALF_A, M_COLS))
R_COLS = M_COLS + ROUTED
PAIR = 2 * ROUTED
AHEAD = 2 * P
LATE = M_COLS - AHEAD
GROUPS = 4
GT = TOKENS // GROUPS
BANK = 512
SCALING = 2.0
LANG_BIAS = 5.0
WARM_UP = 30


def adaln_ffn(nc: bass.Bass, wm, s_late, ar, xt, b2, bias, ids, out):
    with ExitStack() as ctx:
        def sb(name, shape, dt=F32):
            return ctx.enter_context(nc.sbuf_tensor(name, shape, dt))

        def sem(name):
            return ctx.enter_context(nc.semaphore(name))

        wm_f = sb("wm_f", [P, KC, S_EARLY + M_COLS])
        wm_hi = sb("wm_hi", [P, KC, S_EARLY + M_COLS], F32R)
        wm_lo = sb("wm_lo", [P, KC, S_EARLY + M_COLS], F32R)
        late_f = sb("late_f", [P, KC, S_LATE])
        late_hi = sb("late_hi", [P, KC, S_LATE], F32R)
        late_lo = sb("late_lo", [P, KC, S_LATE], F32R)
        ar_f = sb("ar_f", [P, KC, ROUTED])
        b2_f = sb("b2_f", [P, D])
        b2_hi = sb("b2_hi", [P, D], F32R)
        b2_lo = sb("b2_lo", [P, D], F32R)
        bias_all = sb("bias_all", [P, D])
        x_f = sb("x_f", [P, GROUPS, KC, GT])
        x_hi = sb("x_hi", [P, GROUPS, KC, GT], F32R)
        x_lo = sb("x_lo", [P, GROUPS, KC, GT], F32R)
        r_hi = sb("r_hi", [P, KC, R_COLS], F32R)
        r_lo = sb("r_lo", [P, KC, R_COLS], F32R)
        bm_hi = sb("bm_hi", [P, M_COLS], F32R)
        bm_lo = sb("bm_lo", [P, M_COLS], F32R)
        narrow = sb("narrow", [P, TILES, PAIR])
        hg = sb("hg", [P, TILES, ER])
        hgt_hi = [sb(f"hgt{n}_hi", [P, TOKENS], F32R) for n in (1, 2)]
        hgt_lo = [sb(f"hgt{n}_lo", [P, TOKENS], F32R) for n in (1, 2)]
        ids_all = sb("ids_all", [P, TILES], I32)
        expert = sb("expert", [P, TILES, E], I32)
        is_lang = sb("is_lang", [P, TILES, E])
        not_first = sb("not_first", [P, TILES, E])
        logits = sb("logits", [P, TILES, E])
        top = sb("top", [P, TILES, 8])
        at_second = sb("at_second", [P, TILES, E])
        nth_equal = sb("nth_equal", [P, TILES, E])
        tied = sb("tied", [P, TILES])
        chosen = sb("chosen", [P, TILES, E])
        above = sb("above", [P, TILES, E])
        below_max = sb("below_max", [P, TILES, E])
        exps = sb("exps", [P, TILES, E])
        total = sb("total", [P, TILES])
        gates = sb("gates", [P, TILES, E])
        ident = sb("ident", [P, P])
        zeros = sb("zeros", [P, P], BF16)
        sums = x_f[:, :, :, :].rearrange("p g k t -> p (g k t)").rearrange("p (t o) -> p t o", t=TILES)

        ps = ctx.enter_context(nc.psum_tensor("ps", [P, 8, BANK], F32))

        wm_in = [sem(f"wm_in{k}") for k in range(KC)]
        m0_in = [sem("m0_a_in"), sem("m0_b_in")]
        late_in = sem("late_in")
        ar_in, b2_in, bias_in, ids_in = sem("ar_in"), sem("b2_in"), sem("bias_in"), sem("ids_in")
        x_in = [sem(f"x_in{g}") for g in range(GROUPS)]
        wm_hi_done, wm_lo_done = sem("wm_hi_done"), sem("wm_lo_done")
        late_hi_done, late_lo_done = sem("late_hi_done"), sem("late_lo_done")
        ar_hi_done, ar_lo_done = sem("ar_hi_done"), sem("ar_lo_done")
        x_hi_done, x_lo_done = sem("x_hi_done"), sem("x_lo_done")
        b2_hi_done, b2_lo_done = sem("b2_hi_done"), sem("b2_lo_done")
        c_hi_done, c_lo_done = sem("c_hi_done"), sem("c_lo_done")
        hgt_hi_done, hgt_lo_done = sem("hgt_hi_done"), sem("hgt_lo_done")
        c_summed, c_plus_i = sem("c_summed"), sem("c_plus_i")
        narrow_summed, narrow_copied = sem("narrow_summed"), sem("narrow_copied")
        base_summed, base_copied = sem("base_summed"), sem("base_copied")
        hg_turned, second_summed = sem("hg_turned"), sem("second_summed")
        second_added, late_added = sem("second_added"), sem("late_added")
        lora_summed, tile_done = sem("lora_summed"), sem("tile_done")
        bias_put = sem("bias_put")
        zeros_set, ident_zeroed, ident_set, expert_set = (sem("zeros_set"), sem("ident_zeroed"),
                                                          sem("ident_set"), sem("expert_set"))
        route_step, below_max_done, exps_done, hg_done = (sem("route_step"), sem("below_max_done"),
                                                          sem("exps_done"), sem("hg_done"))
        stored = sem("stored")

        m_at = [S_EARLY + lo for lo, _ in HALVES] + [S_EARLY + M_COLS]
        pieces = [(0, 0, S_EARLY), (0, m_at[0], m_at[1]), (0, m_at[1], m_at[2])]
        for k in range(1, KC):
            pieces += [(k, 0, S_EARLY), (k, S_EARLY, S_EARLY + M_COLS)]
        low_order = [1, 2, 0] + [n for k in range(1, KC) for n in (2 * k + 2, 2 * k + 1)]

        def pieces_to(k):
            return 2 * k + 3

        block_banks = [(0, 1), (2, 3), (4, 5), (6, 7), (0, 1)]
        narrow_banks = (2, 3)
        wide_banks = (4, 5, 6, 7)
        turned_banks = ((0, 1), (2, 3))
        PER_TURN = BANK // P
        second_banks = (2, 3, 0, 1)
        PER_SECOND = BANK // AHEAD
        STAY = len(wide_banks)
        lora_order = [*range(STAY, TILES), *range(STAY - 1)]
        LAST_HALVES = ((0, D // 2), (D // 2, D))
        last_banks = (wide_banks[-1], 0)

        block = ctx.enter_context(nc.Block())

        @block.sync
        def _(sp):
            sp.dma_start(wm_f[:, 0, 0:S_EARLY], wm[0, :, 0:S_EARLY]).then_inc(wm_in[0], 16)
            for h in range(2):
                sp.dma_start(wm_f[:, 0, m_at[h]:m_at[h + 1]], wm[0, :, m_at[h]:m_at[h + 1]]).then_inc(m0_in[h], 16)
            for k in range(1, KC):
                sp.dma_start(wm_f[:, k, :], wm[k]).then_inc(wm_in[k], 16)
            sp.dma_start(late_f[:, :, :], s_late).then_inc(late_in, 16)
            sp.dma_start(x_f[:, 0], xt[0]).then_inc(x_in[0], 16)
            sp.dma_start(ar_f[:, :, :], ar).then_inc(ar_in, 16)
            for g in range(1, GROUPS):
                sp.dma_start(x_f[:, g], xt[g]).then_inc(x_in[g], 16)
            sp.dma_start(ids_all[:, :], ids.to_broadcast([P, TILES])).then_inc(ids_in, 16)
            sp.dma_start(bias_all[:, :], bias.to_broadcast([P, D])).then_inc(bias_in, 16)
            sp.dma_start(b2_f[:, :], b2).then_inc(b2_in, 16)
            for n, t in enumerate(lora_order):
                sp.wait_ge(tile_done, n + 1)
                sp.dma_start(out[t], sums[:, t, :]).then_inc(stored, 16)
            for h, (a, b) in enumerate(LAST_HALVES):
                sp.wait_ge(tile_done, TILES + h)
                sp.dma_start(out[STAY - 1, :, a:b], sums[:, STAY - 1, a:b]).then_inc(stored, 16)
            sp.wait_ge(stored, 16 * (TILES + 1))

        @block.gpsimd
        def _(pool):
            nc.gpsimd.memset(ident[:, :], 0.0).then_inc(ident_zeroed, 1)
            nc.gpsimd.iota(expert[:, :, :], pattern=[[0, TILES], [1, E]], base=0,
                           channel_multiplier=0).then_inc(expert_set, 1)
            pool.wait_ge(ident_zeroed, 1)
            nc.gpsimd.affine_select(out=ident[:, :], in_=ident[:, :], compare_op=ALU.not_equal, fill=1.0,
                                    base=0, pattern=[[-1, P]], channel_multiplier=1).then_inc(ident_set, 1)

        @block.scalar
        def _(act):
            for n, (k, a, b) in enumerate(pieces):
                act.wait_ge(m0_in[n - 1] if n in (1, 2) else wm_in[k], 16)
                nc.scalar.copy(wm_hi[:, k, a:b], wm_f[:, k, a:b]).then_inc(wm_hi_done, 1)
            act.wait_ge(late_in, 16)
            nc.scalar.copy(late_hi[:, :, :], late_f[:, :, :]).then_inc(late_hi_done, 1)

            def x_high(g):
                act.wait_ge(x_in[g], 16)
                nc.scalar.copy(x_hi[:, g], x_f[:, g]).then_inc(x_hi_done, 1)

            def c_high(b):
                if b < KC:
                    act.wait_ge(c_plus_i, b + 1)
                else:
                    act.wait_ge(c_summed, b + 1)
                for bank, (lo, hi) in zip(block_banks[b], HALVES):
                    dst = r_hi[:, b, lo:hi] if b < KC else bm_hi[:, lo:hi]
                    nc.scalar.copy(dst, ps[:, bank, 0:hi - lo]).then_inc(c_hi_done, 1)

            x_high(0)
            act.wait_ge(ar_in, 16)
            nc.scalar.copy(r_hi[:, :, M_COLS:], ar_f[:, :, :]).then_inc(ar_hi_done, 1)
            for b in range(KC):
                c_high(b)
            for g in range(1, GROUPS):
                x_high(g)
            c_high(KC)
            for t in range(TILES):
                act.wait_ge(narrow_summed, t + 1)
                nc.scalar.copy(narrow[:, t, :], ps[:, narrow_banks[t % 2], 0:PAIR]).then_inc(narrow_copied, 1)
            act.wait_ge(b2_in, 16)
            nc.scalar.copy(b2_hi[:, :], b2_f[:, :]).then_inc(b2_hi_done, 1)
            act.wait_ge(bias_in, 16)
            act.wait_ge(x_lo_done, GROUPS)
            nc.scalar.copy(sums[:, STAY:, 0:LATE],
                           bias_all[:, 0:LATE].unsqueeze(1).to_broadcast([P, TILES - STAY, LATE])
                           ).then_inc(bias_put, 1)
            for n in range(2):
                act.wait_ge(below_max_done, n + 1)
                nc.scalar.activation(exps[:, :, :], below_max[:, :, :], ACT.Exp).then_inc(exps_done, 1)
                for q in range(2):
                    act.wait_ge(hg_turned, 2 * n + q + 1)
                    nc.scalar.copy(hgt_hi[n][:, q * BANK:(q + 1) * BANK],
                                   ps[:, turned_banks[n][q], :]).then_inc(hgt_hi_done, 1)

        @block.vector
        def _(dve):
            nc.vector.memset(zeros[:, :], 0.0).then_inc(zeros_set, 1)
            for n in low_order:
                k, a, b = pieces[n]
                dve.wait_ge(wm_hi_done, n + 1)
                nc.vector.tensor_tensor(wm_lo[:, k, a:b], wm_f[:, k, a:b],
                                        wm_hi[:, k, a:b].bitcast(F32), ALU.subtract).then_inc(wm_lo_done, 1)
            dve.wait_ge(late_hi_done, 1)
            nc.vector.tensor_tensor(late_lo[:, :, :], late_f[:, :, :], late_hi[:, :, :].bitcast(F32),
                                    ALU.subtract).then_inc(late_lo_done, 1)

            def x_low(g):
                dve.wait_ge(x_hi_done, g + 1)
                nc.vector.tensor_tensor(x_lo[:, g], x_f[:, g], x_hi[:, g].bitcast(F32),
                                        ALU.subtract).then_inc(x_lo_done, 1)

            def c_low(b):
                banks = block_banks[b]
                if b < KC:
                    dve.wait_ge(c_summed, b + 1)
                    half = 0 if b * P < HALF_A else 1
                    at = b * P - HALVES[half][0]
                    diagonal = ps[:, banks[half], at:at + P]
                    nc.vector.tensor_tensor(diagonal, diagonal, ident[:, :], ALU.add).then_inc(c_plus_i, 1)
                for h, (bank, (lo, hi)) in enumerate(zip(banks, HALVES)):
                    high = r_hi[:, b, lo:hi] if b < KC else bm_hi[:, lo:hi]
                    low = r_lo[:, b, lo:hi] if b < KC else bm_lo[:, lo:hi]
                    dve.wait_ge(c_hi_done, 2 * b + h + 1)
                    nc.vector.tensor_tensor(low, ps[:, bank, 0:hi - lo], high.bitcast(F32),
                                            ALU.subtract).then_inc(c_lo_done, 1)

            x_low(0)
            dve.wait_ge(ar_hi_done, 1)
            nc.vector.tensor_tensor(r_lo[:, :, M_COLS:], ar_f[:, :, :], r_hi[:, :, M_COLS:].bitcast(F32),
                                    ALU.subtract).then_inc(ar_lo_done, 1)
            dve.wait_ge(ident_set, 1)
            for b in range(KC):
                c_low(b)
            for g in range(1, GROUPS):
                x_low(g)
            c_low(KC)
            steps = [0]

            def then(ins):
                steps[0] += 1
                ins.then_inc(route_step, 1)
                dve.wait_ge(route_step, steps[0])

            def per_tile(a):
                return a.to_broadcast([P, TILES, E])

            dve.wait_ge(expert_set, 1)
            dve.wait_ge(ids_in, 16)
            nc.vector.tensor_scalar(not_first[:, :, :], expert[:, :, :], 0.0, None, ALU.is_gt)
            then(nc.vector.tensor_tensor(is_lang[:, :, :], expert[:, :, :],
                                         per_tile(ids_all[:, :].unsqueeze(2)), ALU.is_equal))

            def route(n):
                for t in range(TILES):
                    last = nc.vector.max(top[:, t, :], logits[:, t, :])
                then(last)
                first, second = per_tile(top[:, :, 0:1]), per_tile(top[:, :, 1:2])
                nc.vector.tensor_tensor(below_max[:, :, :], logits[:, :, :], first,
                                        ALU.subtract).then_inc(below_max_done, 1)
                nc.vector.tensor_tensor(tied[:, :].unsqueeze(2), top[:, :, 0:1], top[:, :, 1:2], ALU.is_equal)
                nc.vector.tensor_tensor(above[:, :, :], logits[:, :, :], second, ALU.is_gt)
                then(nc.vector.tensor_tensor(at_second[:, :, :], logits[:, :, :], second, ALU.is_equal))
                flat = "p t e -> p (t e)"
                then(nc.vector.tensor_tensor_scan(
                    nth_equal[:, :, :].rearrange(flat), not_first[:, :, :].rearrange(flat),
                    at_second[:, :, :].rearrange(flat), 0.0, ALU.mult, ALU.add))
                then(nc.vector.scalar_tensor_tensor(chosen[:, :, :], nth_equal[:, :, :], -1.0,
                                                    per_tile(tied[:, :].unsqueeze(2)), ALU.add, ALU.is_le))
                then(nc.vector.tensor_tensor(chosen[:, :, :], chosen[:, :, :], at_second[:, :, :], ALU.mult))
                then(nc.vector.tensor_tensor(chosen[:, :, :], chosen[:, :, :], above[:, :, :], ALU.add))
                dve.wait_ge(exps_done, n + 1)
                then(nc.vector.tensor_tensor(chosen[:, :, :], chosen[:, :, :], exps[:, :, :], ALU.mult))
                then(nc.vector.tensor_reduce(total[:, :], chosen[:, :, :], AX_X, ALU.add))
                then(nc.vector.reciprocal(total[:, :], total[:, :]))
                then(nc.vector.scalar_tensor_tensor(gates[:, :, :], chosen[:, :, :], SCALING,
                                                    per_tile(total[:, :].unsqueeze(2)), ALU.mult, ALU.mult))

            def gated(n, first_col):
                for q in range(2):
                    t0, t1 = q * PER_TURN, (q + 1) * PER_TURN
                    if n:
                        dve.wait_ge(hg_turned, q + 1)
                    h = narrow[:, t0:t1, first_col:first_col + ER].rearrange("p t (e r) -> p t e r", e=E)
                    nc.vector.tensor_tensor(
                        hg[:, t0:t1, :].rearrange("p t (e r) -> p t e r", e=E), h,
                        gates[:, t0:t1, :].unsqueeze(3).to_broadcast([P, PER_TURN, E, R]),
                        ALU.mult).then_inc(hg_done, 1)

            def hgt_low(n):
                for q in range(2):
                    cols = slice(q * BANK, (q + 1) * BANK)
                    dve.wait_ge(hgt_hi_done, 2 * n + q + 1)
                    nc.vector.tensor_tensor(hgt_lo[n][:, cols], ps[:, turned_banks[n][q], :],
                                            hgt_hi[n][:, cols].bitcast(F32), ALU.subtract).then_inc(hgt_lo_done, 1)

            def base_out(t):
                dve.wait_ge(base_summed, t + 1)
                nc.vector.tensor_tensor(sums[:, t, :], ps[:, wide_banks[t % STAY], :], bias_all[:, :],
                                        ALU.add).then_inc(base_copied, 1)

            dve.wait_ge(narrow_copied, TILES)
            then(nc.vector.scalar_tensor_tensor(logits[:, :, :], is_lang[:, :, :], LANG_BIAS,
                                                narrow[:, :, ROUTED + ER:], ALU.mult, ALU.add))
            route(0)
            gated(0, ROUTED)
            dve.wait_ge(bias_in, 16)
            dve.wait_ge(x_lo_done, GROUPS)
            base_out(0)
            hgt_low(0)
            for t in range(1, STAY):
                base_out(t)
            dve.wait_ge(b2_hi_done, 1)
            nc.vector.tensor_tensor(b2_lo[:, :], b2_f[:, :], b2_hi[:, :].bitcast(F32),
                                    ALU.subtract).then_inc(b2_lo_done, 1)
            for n in range(TILES // PER_SECOND):
                tiles = slice(n * PER_SECOND, (n + 1) * PER_SECOND)
                dve.wait_ge(second_summed, n + 1)
                part = ps[:, second_banks[n], :].rearrange("p (t c) -> p t c", c=AHEAD)
                mine = narrow[:, tiles, 0:ROUTED]
                nc.vector.tensor_tensor(mine, part[:, :, D - LATE:], mine, ALU.add).then_inc(second_added, 1)
            dve.wait_ge(second_added, TILES // PER_SECOND)
            then(nc.vector.tensor_copy(logits[:, :, :], narrow[:, :, ER:ROUTED]))
            route(1)
            gated(1, 0)
            dve.wait_ge(base_copied, STAY)
            for n in range(TILES // PER_SECOND):
                tiles = slice(n * PER_SECOND, (n + 1) * PER_SECOND)
                part = ps[:, second_banks[n], :].rearrange("p (t c) -> p t c", c=AHEAD)
                on = (sums[:, tiles, LATE:] if n * PER_SECOND < STAY else
                      bias_all[:, LATE:].unsqueeze(1).to_broadcast([P, PER_SECOND, D - LATE]))
                nc.vector.tensor_tensor(sums[:, tiles, LATE:], part[:, :, 0:D - LATE], on,
                                        ALU.add).then_inc(late_added, 1)
            hgt_low(1)
            dve.wait_ge(bias_put, 1)
            dve.wait_ge(late_added, TILES // PER_SECOND)
            for n, t in enumerate(lora_order):
                dve.wait_ge(lora_summed, n + 1)
                nc.vector.tensor_tensor(sums[:, t, :], ps[:, wide_banks[t % STAY], :], sums[:, t, :],
                                        ALU.add).then_inc(tile_done, 1)
            for h, (a, b) in enumerate(LAST_HALVES):
                dve.wait_ge(lora_summed, TILES + h)
                nc.vector.tensor_tensor(sums[:, STAY - 1, a:b], ps[:, last_banks[h], 0:b - a],
                                        sums[:, STAY - 1, a:b], ALU.add).then_inc(tile_done, 1)

        @block.tensor
        def _(pe):
            pe.wait_ge(zeros_set, 1)
            for _ in range(WARM_UP):
                nc.tensor.matmul(ps[:, 7, 0:P], zeros[:, :], zeros[:, :], start=True, stop=True)

            def folding(b, k, low_s, low_m, first, last, halves=(0, 1)):
                if b < EARLY:
                    s = (wm_lo if low_s else wm_hi)[:, k, b * P:(b + 1) * P]
                else:
                    s = (late_lo if low_s else late_hi)[:, k, (b - EARLY) * P:(b - EARLY + 1) * P]
                m = wm_lo if low_m else wm_hi
                for h in halves:
                    lo, hi = HALVES[h]
                    mm = nc.tensor.matmul(ps[:, block_banks[b][h], 0:hi - lo], s,
                                          m[:, k, S_EARLY + lo:S_EARLY + hi], start=first, stop=last)
                if last:
                    mm.then_inc(c_summed, 1)

            passes = ((False, False), (False, True), (True, False))

            for h in range(2):
                pe.wait_ge(wm_hi_done, 2 + h)
                for b in range(EARLY):
                    folding(b, 0, False, False, True, False, (h,))
            for k in range(KC):
                if k:
                    pe.wait_ge(wm_hi_done, pieces_to(k))
                    if k < KC - 1:
                        for b in range(EARLY):
                            folding(b, k, False, False, False, False)
                if k < KC - 1:
                    pe.wait_ge(wm_lo_done, pieces_to(k) - 1)
                    for b in range(EARLY):
                        folding(b, k, False, True, False, False)
                    pe.wait_ge(wm_lo_done, pieces_to(k))
                    for b in range(EARLY):
                        folding(b, k, True, False, False, False)
                else:
                    pe.wait_ge(wm_lo_done, pieces_to(k))
                    for b in range(EARLY):
                        for n, (low_s, low_m) in enumerate(passes):
                            folding(b, k, low_s, low_m, False, n == 2)
            pe.wait_ge(late_lo_done, 1)
            for b in (3, 4):
                if b == 4:
                    pe.wait_ge(c_lo_done, 2)
                for k in range(KC):
                    for n, (low_s, low_m) in enumerate(passes):
                        folding(b, k, low_s, low_m, k == 0 and n == 0, k == KC - 1 and n == 2)

            def x_part(part, t, k):
                g, at = t * P // GT, t * P % GT
                return part[:, g, k, at:at + P]

            def x_product(dst, t, a, b, more=False):
                for k in range(KC):
                    if t == 0:
                        pe.wait_ge(c_lo_done, 2 * (k + 1))
                    for n, (low_x, low_r) in enumerate(passes):
                        mm = nc.tensor.matmul(dst, x_part(x_lo if low_x else x_hi, t, k),
                                              (r_lo if low_r else r_hi)[:, k, a:b],
                                              start=(k == 0 and n == 0), stop=(not more and k == KC - 1 and n == 2))
                return mm

            pe.wait_ge(ar_lo_done, 1)
            for t in range(TILES):
                if t % 2 == 0:
                    pe.wait_ge(x_lo_done, t // 2 + 1)
                if t < 2:
                    pe.wait_ge(c_lo_done, 4)
                else:
                    pe.wait_ge(narrow_copied, t - 1)
                x_product(ps[:, narrow_banks[t % 2], 0:PAIR], t, D, R_COLS).then_inc(narrow_summed, 1)

            def base(t):
                if t < 4:
                    pe.wait_ge(c_lo_done, 2 * KC)
                else:
                    pe.wait_ge(base_copied, t - 3)
                mm = x_product(ps[:, wide_banks[t % STAY], :], t, 0, D, more=(t >= STAY))
                if t < STAY:
                    mm.then_inc(base_summed, 1)

            def turn(n, q):
                pe.wait_ge(hg_done, 2 * n + q + 1)
                if n == 0:
                    pe.wait_ge(c_lo_done, 2 * BLOCKS)
                else:
                    pe.wait_ge(late_added, 2)
                for t in range(q * PER_TURN, (q + 1) * PER_TURN):
                    at = (t % PER_TURN) * P
                    mm = nc.tensor.transpose(ps[:, turned_banks[n][q], at:at + P], hg[:, t, :], ident[:, :])
                mm.then_inc(hg_turned, 1)

            def hgt_product(dst, n, t, high, low, first, last):
                for i, (low_h, low_m) in enumerate(passes):
                    mm = nc.tensor.matmul(dst, (hgt_lo if low_h else hgt_hi)[n][:, t * P:(t + 1) * P],
                                          low if low_m else high, start=(first and i == 0), stop=(last and i == 2))
                return mm

            for t in range(STAY - 1):
                base(t)
            turn(0, 0)
            turn(0, 1)
            base(STAY - 1)
            pe.wait_ge(narrow_copied, TILES)
            pe.wait_ge(hgt_lo_done, 2)
            for t in range(TILES):
                at = (t % PER_SECOND) * AHEAD
                mm = hgt_product(ps[:, second_banks[t // PER_SECOND], at:at + AHEAD], 0, t,
                                 bm_hi[:, LATE:], bm_lo[:, LATE:], True, True)
                if (t + 1) % PER_SECOND == 0:
                    mm.then_inc(second_summed, 1)
            for t in range(STAY, TILES):
                base(t)
            turn(1, 0)
            turn(1, 1)

            def from_hg1(t, first, last):
                return hgt_product(ps[:, wide_banks[t % STAY], 0:LATE], 0, t,
                                   bm_hi[:, 0:LATE], bm_lo[:, 0:LATE], first, last)

            def from_hg2(t, first, last):
                return hgt_product(ps[:, wide_banks[t % STAY], :], 1, t, b2_hi[:, :], b2_lo[:, :], first, last)

            for t in range(STAY, TILES):
                from_hg1(t, False, False)
            pe.wait_ge(b2_lo_done, 1)
            for t in range(STAY, TILES):
                pe.wait_ge(hgt_lo_done, 3 + t // PER_TURN)
                from_hg2(t, False, True).then_inc(lora_summed, 1)
            for t in range(STAY - 1):
                pe.wait_ge(tile_done, t + 1)
                from_hg2(t, True, False)
                from_hg1(t, False, True).then_inc(lora_summed, 1)
            for h, (a, b) in enumerate(LAST_HALVES):
                if h == 0:
                    pe.wait_ge(tile_done, STAY)
                dst = last_banks[h]
                hgt_product(ps[:, dst, 0:b - a], 1, STAY - 1, b2_hi[:, a:b], b2_lo[:, a:b], True, False)
                end = min(b, LATE)
                hgt_product(ps[:, dst, 0:end - a], 0, STAY - 1, bm_hi[:, a:end], bm_lo[:, a:end],
                            False, True).then_inc(lora_summed, 1)


def kernel(x, itok_B_0_7, L0_cond_W, L0_cond_Wr, L0_cond_A, L0_cond_B, L0_ffn_W_base, L0_ffn_b_base,
           L0_ffn_W_router, L0_ffn_lora_A, L0_ffn_lora_B):
    import numpy as np
    import concourse.bacc as bacc
    from concourse.bass_utils import run_bass_kernel_spmd

    def a(v):
        return np.asarray(v)

    w = a(L0_cond_W)
    b1_rows = a(L0_cond_B).transpose(1, 0, 2).reshape(D, ER)
    wm = np.concatenate([w[:, :S_EARLY], a(L0_ffn_W_base).T, a(L0_ffn_lora_A).reshape(ER, D).T,
                         a(L0_ffn_W_router).T], axis=1)
    s_late = np.concatenate([w[:, S_EARLY:], b1_rows], axis=1)
    ar = np.concatenate([a(L0_cond_A).reshape(ER, D).T, a(L0_cond_Wr).T], axis=1)
    arrays = {
        "wm": wm.reshape(KC, P, S_EARLY + M_COLS),
        "s_late": s_late.reshape(KC, P, S_LATE).transpose(1, 0, 2),
        "ar": ar.reshape(KC, P, ROUTED).transpose(1, 0, 2),
        "xt": a(x).reshape(GROUPS, GT, KC, P).transpose(0, 3, 2, 1),
        "b2": a(L0_ffn_lora_B).transpose(0, 2, 1).reshape(ER, D),
        "bias": a(L0_ffn_b_base).reshape(1, D),
        "ids": a(itok_B_0_7).reshape(1, TILES),
    }
    arrays = {name: np.ascontiguousarray(v) for name, v in arrays.items()}
    nc = bacc.Bacc("TRN2", target_bir_lowering=False, num_devices=1)
    args = [nc.dram_tensor(name, v.shape, mybir.dt.from_np(v.dtype), kind="ExternalInput").ap()
            for name, v in arrays.items()]
    out = nc.dram_tensor("out", (TILES, P, D), F32, kind="ExternalOutput").ap()
    adaln_ffn(nc, *args, out)
    result = run_bass_kernel_spmd(nc, [arrays], core_ids=[0])
    return result.results[0]["out"]
```
